# Optimizing a Trainium2 kernel written in Bass

```python
import numpy as np
import jax
import jax.numpy as jnp

def _softmax(x, axis=-1):
    return jax.nn.softmax(x, axis=axis)

def _gelu(x):
    return jax.nn.gelu(x, approximate=True)

def _silu(x):
    return jax.nn.silu(x)

def _sigmoid(x):
    return jax.nn.sigmoid(x)

def _layernorm(x, axis=-1, eps=1e-05):
    m = jnp.mean(x, axis=axis, keepdims=True)
    v = jnp.var(x, axis=axis, keepdims=True)
    return (x - m) / jnp.sqrt(v + eps)

def _scatter_add(tgt, idx, src, axis=0):
    return tgt.at[idx].add(src)

def _segment_sum(src, seg, n):
    return jax.ops.segment_sum(src, seg, n)
kernel_name = 'mk_gnn_resnorm_d4_gnn_r8_9418b3'

def setup_inputs(seed: int=0):
    np.random.seed(seed)
    _w = jnp.asarray

    def _rec_inputs():
        import jax
        import jax.numpy as jnp
        _gk = jax.random.key(seed)
        x = -8.776e-05 + 1 * jax.random.normal(jax.random.fold_in(_gk, 1), (1250, 512), jnp.float32)
        src = jax.random.randint(jax.random.fold_in(_gk, 2), (20000,), 0, 1250, jnp.int32)
        dst = jax.random.randint(jax.random.fold_in(_gk, 3), (20000,), 0, 1250, jnp.int32)
        _o = jnp.argsort(dst, stable=True)
        src = src[_o]
        dst = dst[_o]
        node_vec1 = jax.random.uniform(jax.random.fold_in(_gk, 12), (1250, 1), jnp.float32, 0.0, 0.999957)
        return (x, src, dst, node_vec1)
    x, src, dst, node_vec1 = _rec_inputs()

    def _L0_gnn_setup():
        import jax, jax.numpy as jnp
        import numpy as np
        N_NODES = 1250
        IN_F = 512
        OUT_F = 512
        N_EDGES = 20000
        GRID_SIZE = 5
        SPLINE_ORDER = 3
        ALPHA = 0.2

        def _grid():
            step = 2.0 / GRID_SIZE
            return jnp.arange(-SPLINE_ORDER, GRID_SIZE + SPLINE_ORDER + 1, dtype=jnp.float32) * step - 1.0

        def _b_splines(x, grid):
            x = x[..., None]
            bases = ((x >= grid[:-1]) & (x < grid[1:])).astype(x.dtype)
            for p in range(1, SPLINE_ORDER + 1):
                left = (x - grid[:-(p + 1)]) / (grid[p:-1] - grid[:-(p + 1)]) * bases[..., :-1]
                right = (grid[p + 1:] - x) / (grid[p + 1:] - grid[1:-p]) * bases[..., 1:]
                bases = left + right
            return bases
        key = jax.random.key(seed)
        k1, k2, k3, k4, k5, k6 = jax.random.split(key, 6)
        h = jax.random.normal(k1, (N_NODES, IN_F), dtype=jnp.float32)
        edge_index = jax.random.randint(k2, (2, N_EDGES), 0, N_NODES, dtype=jnp.int64)
        xav = float(np.sqrt(2.0 / (IN_F + OUT_F))) * 1.414
        W = jax.random.normal(k3, (IN_F, OUT_F), dtype=jnp.float32) * xav
        a = jax.random.normal(k4, (2 * OUT_F, 1), dtype=jnp.float32) * float(np.sqrt(2.0 / (2 * OUT_F + 1)))
        base_w = jax.random.normal(k5, (OUT_F, IN_F), dtype=jnp.float32) * xav
        n_coef = GRID_SIZE + SPLINE_ORDER
        spline_w = jax.random.normal(k6, (OUT_F, IN_F, n_coef), dtype=jnp.float32) * 0.1
        return {'h': h, 'W': W, 'a': a, 'base_w': base_w, 'spline_w': spline_w, 'edge_index': edge_index}
    _L0_gnn_all = _L0_gnn_setup()
    _L0_gnn_in = {k: v for k, v in _L0_gnn_all.items() if k in ('W', 'a', 'base_w', 'spline_w')}
    del _L0_gnn_all

    def _L1_gnn_setup():
        import jax, jax.numpy as jnp
        import numpy as np
        N = 1250
        DIM = 512
        H = 8
        C = DIM // H
        E = 20000
        NEG_SLOPE = 0.2
        BN_EPS = 1e-05
        key = jax.random.key(seed)
        ks = jax.random.split(key, 8)
        x = jax.random.normal(ks[0], (N, DIM), dtype=jnp.float32)
        edge_index = jax.random.randint(ks[1], (2, E), 0, N, dtype=jnp.int32)
        s = 1.0 / np.sqrt(DIM)
        W_gat = jax.random.normal(ks[2], (DIM, DIM), dtype=jnp.float32) * s
        att_src = jax.random.normal(ks[3], (H, C), dtype=jnp.float32) * s
        att_dst = jax.random.normal(ks[4], (H, C), dtype=jnp.float32) * s
        gat_bias = jnp.zeros((DIM,), dtype=jnp.float32)
        bn_gamma = jnp.ones((DIM,), dtype=jnp.float32)
        bn_beta = jnp.zeros((DIM,), dtype=jnp.float32)
        W_skip = jax.random.normal(ks[5], (DIM, DIM), dtype=jnp.float32) * s
        b_skip = jnp.zeros((DIM,), dtype=jnp.float32)
        return {'x': x, 'edge_index': edge_index, 'W_gat': W_gat, 'att_src': att_src, 'att_dst': att_dst, 'gat_bias': gat_bias, 'bn_gamma': bn_gamma, 'bn_beta': bn_beta, 'W_skip': W_skip, 'b_skip': b_skip}
    _L1_gnn_all = _L1_gnn_setup()
    _L1_gnn_in = {k: v for k, v in _L1_gnn_all.items() if k in ('W_gat', 'att_src', 'att_dst', 'gat_bias', 'bn_gamma', 'bn_beta', 'W_skip', 'b_skip')}
    del _L1_gnn_all

    def _L2_gnn_setup():
        import jax, jax.numpy as jnp
        import numpy as np
        N_NODES = 6250
        N_EDGES = 50000
        IN_DIM = 512
        OUT_DIM = 512
        key = jax.random.key(seed)
        k1, k2, k3, k4 = jax.random.split(key, 4)
        x = jax.random.normal(k1, (N_NODES, IN_DIM), dtype=jnp.float32)
        edge_index = jax.random.randint(k2, (2, N_EDGES), 0, N_NODES, dtype=jnp.int64)
        W = jax.random.normal(k3, (OUT_DIM, IN_DIM), dtype=jnp.float32) / np.sqrt(IN_DIM)
        b = jax.random.normal(k4, (OUT_DIM,), dtype=jnp.float32) * 0.01
        return {'x': x, 'edge_index': edge_index, 'W': W, 'b': b}
    _L2_gnn_all = _L2_gnn_setup()
    _L2_gnn_in = {k: v for k, v in _L2_gnn_all.items() if k in ('W', 'b')}
    del _L2_gnn_all

    def _L3_gnn_setup():
        import jax, jax.numpy as jnp
        import numpy as np
        N_NODES = 40962
        LATENT_DIM = 512
        N_EDGES = 81924
        NUM_BLOCKS = 4
        NUM_HEADS = 4
        NUM_FREQ = 32
        BASE_PERIOD = 16
        NOISE_EMB_DIM = 16
        EPS = 1e-05

        def _cond_layer_norm(x, cond, sw, sb, bw, bb):
            mu = jnp.mean(x, axis=-1, keepdims=True)
            var = jnp.var(x, axis=-1, keepdims=True)
            xn = (x - mu) * jax.lax.rsqrt(var + EPS)
            scale = cond @ sw + sb
            bias = cond @ bw + bb
            return xn * (1.0 + scale) + bias

        def _sparse_attention(x, src, dst, wq, bq, wk, bk, wv, bv, wo, bo):
            N, D = x.shape
            H, Dh = (NUM_HEADS, D // NUM_HEADS)
            q = (x @ wq + bq).reshape(N, H, Dh) * Dh ** (-0.5)
            k = (x @ wk + bk).reshape(N, H, Dh)
            v = (x @ wv + bv).reshape(N, H, Dh)
            scores = jnp.einsum('ehd,ehd->eh', q[src], k[dst])
            smax = jax.ops.segment_max(scores, src, num_segments=N)
            ex = jnp.exp(scores - smax[src])
            denom = jax.ops.segment_sum(ex, src, num_segments=N)
            attn = ex / denom[src]
            out = jax.ops.segment_sum(attn[:, :, None] * v[dst], src, num_segments=N)
            return out.reshape(N, D) @ wo + bo

        def _forward(x, edge_index, noise_levels, f_w1, f_b1, f_w2, f_b2, s1_w, s1_b, b1_w, b1_b, wq, bq, wk, bk, wv, bv, wo, bo, s2_w, s2_b, b2_w, b2_b, m_w1, m_b1, m_w2, m_b2):
            src, dst = (edge_index[0], edge_index[1])
            freqs = jnp.arange(1, NUM_FREQ + 1, dtype=x.dtype) * (2.0 * np.pi / BASE_PERIOD)
            ph = noise_levels * freqs
            emb = jnp.concatenate([jnp.sin(ph), jnp.cos(ph)], axis=-1)
            cond = jax.nn.silu(emb @ f_w1 + f_b1) @ f_w2 + f_b2
            for i in range(NUM_BLOCKS):
                y = _cond_layer_norm(x, cond, s1_w[i], s1_b[i], b1_w[i], b1_b[i])
                y = _sparse_attention(y, src, dst, wq[i], bq[i], wk[i], bk[i], wv[i], bv[i], wo[i], bo[i])
                x = x + y
                y = _cond_layer_norm(x, cond, s2_w[i], s2_b[i], b2_w[i], b2_b[i])
                y = jax.nn.relu(y @ m_w1[i] + m_b1[i]) @ m_w2[i] + m_b2[i]
                x = x + y
            return x
        key = jax.random.key(seed)
        ks = jax.random.split(key, 20)

        def w(k, shape, s=0.02):
            return jax.random.normal(k, shape, dtype=jnp.float32) * s
        D, B, C = (LATENT_DIM, NUM_BLOCKS, NOISE_EMB_DIM)
        z = lambda *s: jnp.zeros(s, jnp.float32)
        return {'latent_mesh_nodes': jax.random.normal(ks[0], (N_NODES, D), dtype=jnp.float32), 'edge_index': jax.random.randint(ks[1], (2, N_EDGES), 0, N_NODES, dtype=jnp.int32), 'noise_levels': jax.random.uniform(ks[2], (N_NODES, 1), dtype=jnp.float32), 'f_w1': w(ks[3], (2 * NUM_FREQ, C)), 'f_b1': z(C), 'f_w2': w(ks[4], (C, C)), 'f_b2': z(C), 's1_w': w(ks[5], (B, C, D)), 's1_b': z(B, D), 'b1_w': w(ks[6], (B, C, D)), 'b1_b': z(B, D), 'wq': w(ks[7], (B, D, D)), 'bq': z(B, D), 'wk': w(ks[8], (B, D, D)), 'bk': z(B, D), 'wv': w(ks[9], (B, D, D)), 'bv': z(B, D), 'wo': w(ks[10], (B, D, D)), 'bo': z(B, D), 's2_w': w(ks[11], (B, C, D)), 's2_b': z(B, D), 'b2_w': w(ks[12], (B, C, D)), 'b2_b': z(B, D), 'm_w1': w(ks[13], (B, D, D)), 'm_b1': z(B, D), 'm_w2': w(ks[14], (B, D, D)), 'm_b2': z(B, D)}
    _L3_gnn_all = _L3_gnn_setup()
    _L3_gnn_in = {k: v for k, v in _L3_gnn_all.items() if k in ('f_w1', 'f_b1', 'f_w2', 'f_b2', 's1_w', 's1_b', 'b1_w', 'b1_b', 'wq', 'bq', 'wk', 'bk', 'wv', 'bv', 'wo', 'bo', 's2_w', 's2_b', 'b2_w', 'b2_b', 'm_w1', 'm_b1', 'm_w2', 'm_b2')}
    del _L3_gnn_all
    return {'x': x, 'src': src, 'dst': dst, 'node_vec1': node_vec1, 'L0_gnn_W': _L0_gnn_in['W'], 'L0_gnn_a': _L0_gnn_in['a'], 'L0_gnn_base_w': _L0_gnn_in['base_w'], 'L0_gnn_spline_w': _L0_gnn_in['spline_w'], 'L1_gnn_W_gat': _L1_gnn_in['W_gat'], 'L1_gnn_att_src': _L1_gnn_in['att_src'], 'L1_gnn_att_dst': _L1_gnn_in['att_dst'], 'L1_gnn_gat_bias': _L1_gnn_in['gat_bias'], 'L1_gnn_bn_gamma': _L1_gnn_in['bn_gamma'], 'L1_gnn_bn_beta': _L1_gnn_in['bn_beta'], 'L1_gnn_W_skip': _L1_gnn_in['W_skip'], 'L1_gnn_b_skip': _L1_gnn_in['b_skip'], 'L2_gnn_W': _L2_gnn_in['W'], 'L2_gnn_b': _L2_gnn_in['b'], 'L3_gnn_f_w1': _L3_gnn_in['f_w1'], 'L3_gnn_f_b1': _L3_gnn_in['f_b1'], 'L3_gnn_f_w2': _L3_gnn_in['f_w2'], 'L3_gnn_f_b2': _L3_gnn_in['f_b2'], 'L3_gnn_s1_w': _L3_gnn_in['s1_w'], 'L3_gnn_s1_b': _L3_gnn_in['s1_b'], 'L3_gnn_b1_w': _L3_gnn_in['b1_w'], 'L3_gnn_b1_b': _L3_gnn_in['b1_b'], 'L3_gnn_wq': _L3_gnn_in['wq'], 'L3_gnn_bq': _L3_gnn_in['bq'], 'L3_gnn_wk': _L3_gnn_in['wk'], 'L3_gnn_bk': _L3_gnn_in['bk'], 'L3_gnn_wv': _L3_gnn_in['wv'], 'L3_gnn_bv': _L3_gnn_in['bv'], 'L3_gnn_wo': _L3_gnn_in['wo'], 'L3_gnn_bo': _L3_gnn_in['bo'], 'L3_gnn_s2_w': _L3_gnn_in['s2_w'], 'L3_gnn_s2_b': _L3_gnn_in['s2_b'], 'L3_gnn_b2_w': _L3_gnn_in['b2_w'], 'L3_gnn_b2_b': _L3_gnn_in['b2_b'], 'L3_gnn_m_w1': _L3_gnn_in['m_w1'], 'L3_gnn_m_b1': _L3_gnn_in['m_b1'], 'L3_gnn_m_w2': _L3_gnn_in['m_w2'], 'L3_gnn_m_b2': _L3_gnn_in['m_b2']}

def reference(x, src, dst, node_vec1, L0_gnn_W, L0_gnn_a, L0_gnn_base_w, L0_gnn_spline_w, L1_gnn_W_gat, L1_gnn_att_src, L1_gnn_att_dst, L1_gnn_gat_bias, L1_gnn_bn_gamma, L1_gnn_bn_beta, L1_gnn_W_skip, L1_gnn_b_skip, L2_gnn_W, L2_gnn_b, L3_gnn_f_w1, L3_gnn_f_b1, L3_gnn_f_w2, L3_gnn_f_b2, L3_gnn_s1_w, L3_gnn_s1_b, L3_gnn_b1_w, L3_gnn_b1_b, L3_gnn_wq, L3_gnn_bq, L3_gnn_wk, L3_gnn_bk, L3_gnn_wv, L3_gnn_bv, L3_gnn_wo, L3_gnn_bo, L3_gnn_s2_w, L3_gnn_s2_b, L3_gnn_b2_w, L3_gnn_b2_b, L3_gnn_m_w1, L3_gnn_m_b1, L3_gnn_m_w2, L3_gnn_m_b2):
    import jax
    import jax.numpy as jnp

    def _L0_gnn_ref(h, W, a, base_w, spline_w, edge_index):
        import jax, jax.numpy as jnp
        import numpy as np
        N_NODES = 1250
        IN_F = 512
        OUT_F = 512
        N_EDGES = 20000
        GRID_SIZE = 5
        SPLINE_ORDER = 3
        ALPHA = 0.2

        def _grid():
            step = 2.0 / GRID_SIZE
            return jnp.arange(-SPLINE_ORDER, GRID_SIZE + SPLINE_ORDER + 1, dtype=jnp.float32) * step - 1.0

        def _b_splines(x, grid):
            x = x[..., None]
            bases = ((x >= grid[:-1]) & (x < grid[1:])).astype(x.dtype)
            for p in range(1, SPLINE_ORDER + 1):
                left = (x - grid[:-(p + 1)]) / (grid[p:-1] - grid[:-(p + 1)]) * bases[..., :-1]
                right = (grid[p + 1:] - x) / (grid[p + 1:] - grid[1:-p]) * bases[..., 1:]
                bases = left + right
            return bases
        HW = h @ W
        row, col = (edge_index[0], edge_index[1])
        s = HW @ a[:OUT_F, 0]
        t = HW @ a[OUT_F:, 0]
        e = jax.nn.leaky_relu(s[row] + t[col], negative_slope=ALPHA)
        m = jax.ops.segment_max(e, row, num_segments=N_NODES)
        ex = jnp.exp(e - m[row])
        den = jax.ops.segment_sum(ex, row, num_segments=N_NODES)
        att = ex / den[row]
        agg = jax.ops.segment_sum(att[:, None] * h[col], row, num_segments=N_NODES)
        grid = _grid()
        basis = _b_splines(agg, grid)
        out = jax.nn.silu(agg) @ base_w.T + jnp.einsum('nip,oip->no', basis, spline_w)
        return out

    def _L1_gnn_ref(x, edge_index, W_gat, att_src, att_dst, gat_bias, bn_gamma, bn_beta, W_skip, b_skip):
        import jax, jax.numpy as jnp
        import numpy as np
        N = 1250
        DIM = 512
        H = 8
        C = DIM // H
        E = 20000
        NEG_SLOPE = 0.2
        BN_EPS = 1e-05
        identity = x @ W_skip + b_skip
        loops = jnp.arange(N, dtype=edge_index.dtype)
        src = jnp.concatenate([edge_index[0], loops])
        dst = jnp.concatenate([edge_index[1], loops])
        h = (x @ W_gat).reshape(N, H, C)
        a_src = jnp.einsum('nhc,hc->nh', h, att_src)
        a_dst = jnp.einsum('nhc,hc->nh', h, att_dst)
        e = a_src[src] + a_dst[dst]
        e = jnp.where(e >= 0, e, NEG_SLOPE * e)
        m = jax.ops.segment_max(e, dst, num_segments=N)
        ex = jnp.exp(e - m[dst])
        denom = jax.ops.segment_sum(ex, dst, num_segments=N)
        alpha = ex / denom[dst]
        msgs = alpha[:, :, None] * h[src]
        out = jax.ops.segment_sum(msgs, dst, num_segments=N)
        out = out.reshape(N, DIM) + gat_bias
        mean = out.mean(axis=0)
        var = out.var(axis=0)
        out = (out - mean) * jax.lax.rsqrt(var + BN_EPS) * bn_gamma + bn_beta
        out = jax.nn.gelu(out, approximate=False)
        return out + identity

    def _L2_gnn_ref(x, edge_index, W, b):
        import jax, jax.numpy as jnp
        import numpy as np
        N_NODES = 6250
        N_EDGES = 50000
        IN_DIM = 512
        OUT_DIM = 512
        n = x.shape[0]
        loops = jnp.arange(n, dtype=edge_index.dtype)
        row = jnp.concatenate([edge_index[0], loops])
        col = jnp.concatenate([edge_index[1], loops])
        deg = jax.ops.segment_sum(jnp.ones(row.shape[0], dtype=x.dtype), row, num_segments=n)
        dis = jax.lax.rsqrt(deg)
        norm = dis[row] * dis[col]
        h = x @ W.T + b
        out = jax.ops.segment_sum(norm[:, None] * h[row], col, num_segments=n)
        return jax.nn.relu(out)

    def _L3_gnn_ref(latent_mesh_nodes, edge_index, noise_levels, f_w1, f_b1, f_w2, f_b2, s1_w, s1_b, b1_w, b1_b, wq, bq, wk, bk, wv, bv, wo, bo, s2_w, s2_b, b2_w, b2_b, m_w1, m_b1, m_w2, m_b2):
        import jax, jax.numpy as jnp
        import numpy as np
        N_NODES = 40962
        LATENT_DIM = 512
        N_EDGES = 81924
        NUM_BLOCKS = 4
        NUM_HEADS = 4
        NUM_FREQ = 32
        BASE_PERIOD = 16
        NOISE_EMB_DIM = 16
        EPS = 1e-05

        def _cond_layer_norm(x, cond, sw, sb, bw, bb):
            mu = jnp.mean(x, axis=-1, keepdims=True)
            var = jnp.var(x, axis=-1, keepdims=True)
            xn = (x - mu) * jax.lax.rsqrt(var + EPS)
            scale = cond @ sw + sb
            bias = cond @ bw + bb
            return xn * (1.0 + scale) + bias

        def _sparse_attention(x, src, dst, wq, bq, wk, bk, wv, bv, wo, bo):
            N, D = x.shape
            H, Dh = (NUM_HEADS, D // NUM_HEADS)
            q = (x @ wq + bq).reshape(N, H, Dh) * Dh ** (-0.5)
            k = (x @ wk + bk).reshape(N, H, Dh)
            v = (x @ wv + bv).reshape(N, H, Dh)
            scores = jnp.einsum('ehd,ehd->eh', q[src], k[dst])
            smax = jax.ops.segment_max(scores, src, num_segments=N)
            ex = jnp.exp(scores - smax[src])
            denom = jax.ops.segment_sum(ex, src, num_segments=N)
            attn = ex / denom[src]
            out = jax.ops.segment_sum(attn[:, :, None] * v[dst], src, num_segments=N)
            return out.reshape(N, D) @ wo + bo

        def _forward(x, edge_index, noise_levels, f_w1, f_b1, f_w2, f_b2, s1_w, s1_b, b1_w, b1_b, wq, bq, wk, bk, wv, bv, wo, bo, s2_w, s2_b, b2_w, b2_b, m_w1, m_b1, m_w2, m_b2):
            src, dst = (edge_index[0], edge_index[1])
            freqs = jnp.arange(1, NUM_FREQ + 1, dtype=x.dtype) * (2.0 * np.pi / BASE_PERIOD)
            ph = noise_levels * freqs
            emb = jnp.concatenate([jnp.sin(ph), jnp.cos(ph)], axis=-1)
            cond = jax.nn.silu(emb @ f_w1 + f_b1) @ f_w2 + f_b2
            for i in range(NUM_BLOCKS):
                y = _cond_layer_norm(x, cond, s1_w[i], s1_b[i], b1_w[i], b1_b[i])
                y = _sparse_attention(y, src, dst, wq[i], bq[i], wk[i], bk[i], wv[i], bv[i], wo[i], bo[i])
                x = x + y
                y = _cond_layer_norm(x, cond, s2_w[i], s2_b[i], b2_w[i], b2_b[i])
                y = jax.nn.relu(y @ m_w1[i] + m_b1[i]) @ m_w2[i] + m_b2[i]
                x = x + y
            return x
        return _forward(latent_mesh_nodes, edge_index, noise_levels, f_w1, f_b1, f_w2, f_b2, s1_w, s1_b, b1_w, b1_b, wq, bq, wk, bk, wv, bv, wo, bo, s2_w, s2_b, b2_w, b2_b, m_w1, m_b1, m_w2, m_b2)
    edge_index = jnp.stack([src, dst])
    x = _layernorm(x + _L0_gnn_ref(x, L0_gnn_W, L0_gnn_a, L0_gnn_base_w, L0_gnn_spline_w, edge_index), axis=-1)
    x = _layernorm(x + _L1_gnn_ref(x, edge_index, L1_gnn_W_gat, L1_gnn_att_src, L1_gnn_att_dst, L1_gnn_gat_bias, L1_gnn_bn_gamma, L1_gnn_bn_beta, L1_gnn_W_skip, L1_gnn_b_skip), axis=-1)
    x = _layernorm(x + _L2_gnn_ref(x, edge_index, L2_gnn_W, L2_gnn_b), axis=-1)
    x = _layernorm(x + _L3_gnn_ref(x, edge_index, node_vec1, L3_gnn_f_w1, L3_gnn_f_b1, L3_gnn_f_w2, L3_gnn_f_b2, L3_gnn_s1_w, L3_gnn_s1_b, L3_gnn_b1_w, L3_gnn_b1_b, L3_gnn_wq, L3_gnn_bq, L3_gnn_wk, L3_gnn_bk, L3_gnn_wv, L3_gnn_bv, L3_gnn_wo, L3_gnn_bo, L3_gnn_s2_w, L3_gnn_s2_b, L3_gnn_b2_w, L3_gnn_b2_b, L3_gnn_m_w1, L3_gnn_m_b1, L3_gnn_m_w2, L3_gnn_m_b2), axis=-1)
    return x

_drawn_inputs = setup_inputs


def setup_inputs(seed=0):
    import zlib

    import numpy as np

    out = dict(_drawn_inputs(seed))
    spreads = {'L1_gnn_gat_bias': (0.0, 0.8),
     'L1_gnn_bn_gamma': (1.0, 0.2),
     'L1_gnn_bn_beta': (0.0, 0.1),
     'L1_gnn_b_skip': (0.0, 0.1),
     'L3_gnn_f_b1': (0.0, 0.8),
     'L3_gnn_f_b2': (0.0, 0.8),
     'L3_gnn_s1_b': (0.0, 0.579),
     'L3_gnn_b1_b': (0.0, 0.388),
     'L3_gnn_bq': (0.0, 0.8),
     'L3_gnn_bk': (0.0, 0.8),
     'L3_gnn_bv': (0.0, 0.1),
     'L3_gnn_bo': (0.0, 0.1),
     'L3_gnn_s2_b': (0.0, 0.579),
     'L3_gnn_b2_b': (0.0, 0.559),
     'L3_gnn_m_b1': (0.0, 0.1),
     'L3_gnn_m_b2': (0.0, 0.1)}
    factors = {'node_vec1': 8.0,
     'L2_gnn_b': 8.0,
     'L3_gnn_f_w1': 8.0,
     'L3_gnn_f_w2': 8.0,
     'L3_gnn_s1_w': 8.0,
     'L3_gnn_b1_w': 8.0,
     'L3_gnn_wq': 8.0,
     'L3_gnn_wk': 8.0,
     'L3_gnn_s2_w': 8.0,
     'L3_gnn_b2_w': 8.0}
    for name, (base, spread) in spreads.items():
        noise = np.random.default_rng([zlib.crc32(name.encode()), seed]).standard_normal(out[name].shape)
        drawn = base * np.exp(spread * noise) if base else spread * noise
        out[name] = jnp.asarray(drawn.astype(out[name].dtype))
    for name, factor in factors.items():
        out[name] = (out[name] * factor).astype(out[name].dtype)
    return out
```

```python
from contextlib import ExitStack

import numpy as np
import concourse.bass as bass
from concourse import mybir
from concourse.alu_op_type import AluOpType as ALU

F32 = mybir.dt.float32
BF16 = mybir.dt.bfloat16
I32 = mybir.dt.int32
I16 = mybir.dt.int16
ACT = mybir.ActivationFunctionType
AX_X = mybir.AxisListType.X

N, F, E = 1250, 512, 20000
TP = 125
T = N // TP
FC = F // 128
BANK = 512
COLS = [(c, min(BANK, N - c)) for c in range(0, N, BANK)]
GROUPS = [(0, 3), (3, 3), (6, 2), (8, 2)]
NG = len(GROUPS)
GW = 3 * TP
EC = E // TP
U = 4
EB = EC // U
BIG = 1e30
NO_ROW = 1e29
TINY = 1e-15
EPS = 1e-5
SLOPE = 0.2
H1, C1 = 8, F // 8
BLOCKS, HEADS = 4, 4
DH = F // HEADS
QSCALE = float(DH) ** -0.5
HALF = N // 2
HT = T // 2
R = 3
PARTS = {3: (0, (0, 1, 2, 3)), 4: (0, (4, 5, 6)), 5: (0, (7, 8, 9)),
         6: (1, (0, 1, 2, 3)), 7: (1, (4, 5, 6)), 8: (1, (7, 8, 9)), 9: (2, (0, 1, 2, 3))}
VALUE_TILES = ((0, 1, 2, 3), (4, 5, 6, 7), (8, 9))
NB = 9
TWO_PI = 6.283185307179586
PI_PARTS = (6.28125, 0.0019350051879882812, 3.019915981956753e-07)
MAGIC = 12582912.0


def shape_constants():
    freqs = np.zeros((64, 3), np.float32)
    freqs[:, 0] = np.tile(np.arange(1, 33, dtype=np.float32) * np.float32(TWO_PI / 16), 2)
    freqs[32:, 1] = 0.25
    freqs[32:, 2] = np.pi / 2
    feature = np.arange(F).reshape(FC, 128).T
    head_of = (feature[:, :, None] // C1 == np.arange(H1)).astype(np.float32)
    minus_centre = np.tile(3.5 - np.arange(8, dtype=np.float32), (128, 1))
    batch = np.tile(np.arange(EB, dtype=np.float32), T)[None]
    return {
        "ident": np.eye(128, dtype=np.float32), "freqs": freqs, "head_of": head_of,
        "minus_centre": minus_centre, "batch_first": batch - (EB - 1), "batch_end": batch + 1,
    }


def program(nc, a, out):
    ctx = ExitStack()
    with ctx:
        def sb(name, shape, dt=F32):
            return ctx.enter_context(nc.sbuf_tensor(name, shape, dt))

        def sem(name):
            return ctx.enter_context(nc.semaphore(name))

        def scratch(name, shape, dt=F32):
            return nc.dram_tensor(name, shape, dt).ap()

        mask_t_dram = scratch("mask_t_dram", (T, TP, N))
        mask_dram = scratch("mask_dram", (T, TP, N))
        count_loops_dram = scratch("count_loops_dram", (T, TP, N))
        rows_dram = scratch("rows_dram", (1 + H1, N))
        x3_dram = scratch("x3_dram", (TP, T * F))

        X = sb("X", [128, T, F])
        XT = sb("XT", [128, FC, N])
        OT = sb("OT", [128, FC, N])
        M = sb("M", [128, T, N])
        PT = sb("PT", [128, 2 * T * GW + R * N])
        SB = PT[:, 2 * T * GW:].rearrange("p (r n) -> p r n", r=R)
        WS = sb("WS", [128, 3 * FC * F])
        VH = sb("VH", [128, T * DH])
        QK = sb("QK", [128, 2, N])
        condT = sb("condT", [32, N])
        bv_all = sb("bv_all", [128, F])
        ident = sb("ident_sb", [128, 128])
        cols = sb("cols", [128, 192])
        rows = QK[0:1, 1, :]
        tiny = sb("tiny", [128, 1])
        eps = sb("eps", [128, 1])

        pt = PT[:, 0:2 * T * GW].rearrange("p (b j c) -> p b j c", b=2, j=T)
        H = WS[:, 0:T * F].rearrange("p (t f) -> p t f", t=T)
        vh = VH[:, :].rearrange("p (t d) -> p t d", t=T)
        vh1 = VH[:, :].rearrange("p (e t d) -> p e t d", e=2, t=T)
        wslot = [WS[:, FC * F * i:FC * F * (i + 1)].rearrange("p (c f) -> p c f", c=FC) for i in range(3)]
        pslot = [PT[:, FC * F * i:FC * F * (i + 1)].rearrange("p (c f) -> p c f", c=FC) for i in range(3)]

        at = [0]

        def column(n):
            at[0] += n
            return cols[:, at[0] - n:at[0]]

        a_cols = column(8).rearrange("p (c k) -> p c k", c=FC)
        u_cols = column(8).rearrange("p (c k) -> p c k", c=FC)
        neg_s = column(T)
        att_cols = column(8).rearrange("p (k c) -> p k c", k=2)
        gat_bias, gamma, beta = column(FC), column(FC), column(FC)
        centre = column(8)
        shift2, den2, inv2 = column(R), column(R), column(R)
        stats = sb("stats", [128, 12, 6])
        moments = sb("moments", [128, T, 2])
        rstd = column(T)
        dis = column(T)
        bn_scale, bn_shift = column(FC), column(FC)
        neg_bq, bk, bm1 = column(16), column(16), column(16)
        freq = column(3)
        fb1, fb2 = column(1), column(1)
        fw = sb("fw", [64, 32])
        head_of = sb("head_of_sb", [128, FC, H1])
        att16 = sb("att16", [128, FC, 2 * H1])
        u16 = sb("u16", [128, FC, 2 * H1])
        neg_ad = sb("neg_ad", [128, T, H1])
        table = sb("table", [1, 2 * T], I32)

        iota32 = PT[:, 0:N].bitcast(I32)
        iota16 = QK[:, 0, 0:N // 2].bitcast(I16)
        one_src = OT[:, :, :].rearrange("p c n -> p (c n)")[:, 0:U * N // 2].bitcast(BF16).rearrange("p (u n) -> p u n", u=U)
        oth = OT[:, :, :].rearrange("p c n -> p (c n)")
        one_dst = oth[:, 2500:2500 + U * TP // 2].bitcast(BF16).rearrange("p (u n) -> p u n", u=U)
        zero_bf = oth[:, 2800:2800 + BANK // 2].bitcast(BF16)
        ones_bf = oth[:, 3100:3102].bitcast(BF16)
        edge_i = WS[:, 0:2 * EC].bitcast(I32)
        src_f = WS[:, 400:400 + EC]
        dst_f = WS[:, 600:600 + EC]
        ge_bf = WS[:, 800:800 + T * EC // 2].bitcast(BF16).rearrange("p (t k) -> p t k", t=T)
        in_tile = WS[:, 1600:1600 + T * EC // 2].bitcast(BF16).rearrange("p (t k) -> p t k", t=T)
        in_batch = WS[:, 2400:2400 + T * EB // 2].bitcast(BF16)
        ct = [OT[:, 3, :], VH[:, 0:N]]
        gbuf = [PT[:, N * i:N * (i + 1)] for i in range(8)]

        rows_sb = QK[:, 1, :]
        basis = [WS[:, 0:2500], WS[:, 2500:5000], QK[:, :, :].rearrange("p a n -> p (a n)")]
        basis = [v.rearrange("p (c n) -> p c n", c=FC) for v in basis]
        xt_flat = XT[:, :, :].rearrange("p c n -> p (c n)")
        sp_u, sp_a = PT[:, 6144:8644], xt_flat[:, 0:2500]
        sp_a3, sp_b3 = xt_flat[:, 2500:5000], PT[:, 8644:11144]
        bias_row = PT[:, 4096:4096 + F]
        temp = [PT[:, 4608:4608 + F], PT[:, 5120:5120 + F]]
        cond_w = [PT[0:17, 0:F], PT[0:17, F:2 * F]]
        bias3 = PT[:, 2 * F:3 * F]
        xn = [PT[:, F * (3 + i):F * (4 + i)] for i in range(2)]
        yb = [PT[:, F * (5 + i):F * (6 + i)] for i in range(2)]

        psA = ctx.enter_context(nc.psum_tensor("psA", [128, 3 * BANK], F32))
        psB = ctx.enter_context(nc.psum_tensor("psB", [128, 3 * BANK], F32))
        psC = ctx.enter_context(nc.psum_tensor("psC", [128, BANK], F32))
        psD = ctx.enter_context(nc.psum_tensor("psD", [128, BANK], F32))
        acc = [psC, psD]
        blocks_B = psB[:, 0:T * 128].rearrange("p (j c) -> p j c", c=128)

        stage_done, tick = sem("stage_done"), sem("tick")
        const_in, edges_in, x_in = sem("const_in"), sem("edges_in"), sem("x_in")
        iota_done, graph_dve, memb_sum, table_ready = sem("iota_done"), sem("graph_dve"), sem("memb_sum"), sem("table_ready")
        hot_ready = [sem(f"hot_ready{d}") for d in range(T)]
        hot_used = [sem(f"hot_used{d}") for d in range(T)]
        ct_counted, ct_copied, ct_turned, ct_placed = sem("ct_counted"), sem("ct_copied"), sem("ct_turned"), sem("ct_placed")
        loops_step, ln_done, mask_t_ready = sem("loops_step"), sem("ln_done"), sem("mask_t_ready")
        mask_t_out = [sem(f"mask_t_out{i}") for i in range(2)]
        ln2_done, zero2, mask_ready, mask_out, cl_step = (sem(n) for n in ("ln2_done", "zero2", "mask_ready", "mask_out", "cl_step"))
        cl_out = [sem(f"cl_out{i}") for i in range(2)]

        w0_in, u_ready, u_copied, trow_ready, trow_copied, scol_ready, scol_copied, trow_out, trow_in = (
            sem(n) for n in ("w0_in", "u_ready", "u_copied", "trow_ready", "trow_copied", "scol_ready", "scol_copied", "trow_out", "trow_in"))
        raw_ready, shifted, exped, inv_step, prob_ready, turned, placed, acc_ready, acc_taken = (
            sem(n) for n in ("raw_ready", "shifted", "exped", "inv_step", "prob_ready", "turned", "placed", "acc_ready", "acc_taken"))
        mask_in = sem("mask_in")
        sloped = sem("sloped")
        spline_w_in = [sem(f"spline_w_in{i}") for i in range(3)]
        abs_done, cut_done, square_done, cube_done, basis_ready, basis_used = (
            sem(n) for n in ("abs_done", "cut_done", "square_done", "cube_done", "basis_ready", "basis_used"))
        half_added, ln_step = sem("half_added"), sem("ln_step")
        xt_turned, xt_placed = sem("xt_turned"), sem("xt_placed")
        gat_w_in, att_done, u16_ready, u16_copied, h_ready, h_copied, arow_ready, arow_copied, arow_out, ad_ready, ad_done = (
            sem(n) for n in ("gat_w_in", "att_done", "u16_ready", "u16_copied", "h_ready", "h_copied", "arow_ready", "arow_copied", "arow_out", "ad_ready", "ad_done"))
        arow_in = [sem(f"arow_in{i}") for i in range(2)]
        vh1_ready = [sem(f"vh1_ready{i}") for i in range(2)]
        skip_in, bn_step, gelu_done, bias_added, skip_ready, skip_added = (
            sem(n) for n in ("skip_in", "bn_step", "gelu_done", "bias_added", "skip_ready", "skip_added"))
        w2_in, h2_ready, h2_step, h2_done, dis_step, agg_ready, agg_relued, agg_added = (
            sem(n) for n in ("w2_in", "h2_ready", "h2_step", "h2_done", "dis_step", "agg_ready", "agg_relued", "agg_added"))
        noise_in, x3_out, ph_step, sin_done, c1_ready, c1_done, c2_ready, c2_done, x3_in, out_done = (
            sem(n) for n in ("noise_in", "x3_out", "ph_step", "sin_done", "c1_ready", "c1_done", "c2_ready", "c2_done", "x3_in", "out_done"))
        w_in = [sem(f"w_in{i}") for i in range(3)]
        cond_in, bv_in = sem("cond_in"), sem("bv_in")
        cond_ready, y_step, y_ready, bias3_added = sem("cond_ready"), sem("y_step"), sem("y_ready"), sem("bias3_added")
        q_ready, q_done, k_ready, k_done, v_ready, v_done = (sem(n) for n in ("q_ready", "q_done", "k_ready", "k_done", "v_ready", "v_done"))
        proj_ready, proj_added, hid_ready, hid_done = (sem(n) for n in ("proj_ready", "proj_added", "hid_ready", "hid_done"))

        G1, A1 = T, FC * NG
        G3, A3 = T + H1 * T, FC * NG + H1 * NG

        def at_least(e, s, v):
            if not isinstance(v, int) or v > 0:
                e.wait_ge(s, v)

        def slot(i):
            return SB[0:TP, i % R, :]

        def own(v, i):
            return v[0:TP, i % R:i % R + 1]

        def freed(i, per):
            if i >= R:
                return i - R + 1
            return max(j for j in range(per) if j % R == i) - per + 1

        def group_of(t):
            return next(k for k, (first, n) in enumerate(GROUPS) if first <= t < first + n)

        block = ctx.enter_context(nc.Block())

        def settle(e):
            e.sem_inc(tick, 1)

        def stage_end(e, n):
            e.drain().then_inc(stage_done, 1)
            e.wait_ge(stage_done, 5 * n)

        def loop_stage_end(e, b, k):
            e.drain().then_inc(stage_done, 1)
            e.wait_ge(stage_done, b * 25 + 5 * (10 + k))
            e.sem_inc(tick, 1)

        LN3 = 18 + 8 * BLOCKS

        @block.sync
        def _(sp):
            for name, to in (("ident", ident[:, :]), ("head_of", head_of[:, :, :]), ("minus_centre", centre),
                             ("L0_a", a_cols), ("att", att_cols), ("gat_bias", gat_bias), ("gamma", gamma), ("beta", beta),
                             ("batch_first", rows[:, 0:T * EB]), ("batch_end", rows[:, T * EB:2 * T * EB]),
                             ("bq", neg_bq), ("bk", bk), ("bm1", bm1), ("freqs", freq[0:64, :]),
                             ("f_b1", fb1[0:16, :]), ("f_b2", fb2[0:16, :]),
                             ("f_w1", fw[0:64, 0:16]), ("f_w2", fw[0:16, 16:32])):
                sp.dma_start(to, a[name]).then_inc(const_in, 16)
            sp.dma_start(edge_i[0:TP, :], a["edges"]).then_inc(edges_in, 16)
            sp.dma_start(X[0:TP, :, :], a["x"].rearrange("(t p) f -> p t f", p=TP)).then_inc(x_in, 16)
            sp.dma_start(XT[:, :, :], a["xT"].rearrange("(c p) n -> p c n", p=128)).then_inc(x_in, 16)
            for d in range(T):
                sp.wait_ge(mask_t_ready, d + 1)
                sp.dma_start(mask_t_dram[d], gbuf[6 + d % 2][0:TP, :]).then_inc(mask_t_out[d % 2], 16)
            for s in mask_t_out:
                sp.wait_ge(s, 16 * (T // 2))
            stage_end(sp, 1)
            for t in range(T):
                sp.wait_ge(cl_step, 2 * (t + 1))
                sp.dma_start(count_loops_dram[t], gbuf[4 + t % 2][0:TP, :]).then_inc(cl_out[t % 2], 16)
                sp.wait_ge(mask_ready, t + 1)
                sp.dma_start(mask_dram[t], M[0:TP, t, :]).then_inc(mask_out, 16)
            for s in cl_out:
                sp.wait_ge(s, 16 * (T // 2))
            sp.wait_ge(mask_out, 16 * T)
            sp.dma_start(wslot[0], a["L0_WT"].rearrange("(c p) f -> p c f", p=128)).then_inc(w0_in, 16)
            stage_end(sp, 2)
            sp.wait_ge(trow_copied, 1)
            sp.dma_start(rows_dram[0:1, :], QK[0:1, 1, :]).then_inc(trow_out, 16)
            sp.wait_ge(trow_out, 16)
            sp.dma_start(QK[0:TP, 0, :], rows_dram[0].partition_broadcast(TP)).then_inc(trow_in, 16)
            stage_end(sp, 3)
            sp.dma_start(M[0:TP, :, :], mask_t_dram.rearrange("t p n -> p t n")).then_inc(mask_in, 16)
            for i in range(3):
                sp.dma_start(pslot[i], a["spline_w"][i]).then_inc(spline_w_in[i], 16)
            with sp.Fori(0, 2) as half:
                for k in range(NB):
                    if k < NB - 3:
                        sp.wait_ge(basis_used, half * NB + (k + 3))
                        sp.dma_start(pslot[k % 3], a["spline_w"][k + 3]).then_inc(spline_w_in[k % 3], 16)
                    else:
                        sp.wait_ge(basis_used, half * NB + (k + 3))
                        sp.dma_start(pslot[k % 3], a["spline_w"][k + 3 - NB]).then_inc(spline_w_in[k % 3], 16)
            for i in range(3):
                sp.wait_ge(spline_w_in[i], 16 * 7)
            stage_end(sp, 4)
            sp.dma_start(pslot[0], a["W_gat"].rearrange("(c p) f -> p c f", p=128)).then_inc(gat_w_in, 16)
            sp.dma_start(pslot[1], a["W_gatT"].rearrange("(c p) f -> p c f", p=128)).then_inc(gat_w_in, 16)
            sp.wait_ge(arow_copied, 1)
            sp.dma_start(rows_dram[1:1 + H1, :], QK[0:H1, 0, :]).then_inc(arow_out, 16)
            sp.wait_ge(arow_out, 16)
            stage_end(sp, 5)
            with sp.Fori(0, H1 // 2) as pair:
                for e in range(2):
                    sp.wait_ge(raw_ready, pair * (2 * T) + T * e + (2 if e == 0 else 0))
                    sp.dma_start(QK[0:TP, e, :], rows_dram[bass.ds(pair * 2 + (1 + e), 1), :].rearrange("a n -> (a n)").partition_broadcast(TP)).then_inc(arow_in[e], 16)
            stage_end(sp, 6)
            sp.dma_start(M[0:TP, :, :], count_loops_dram.rearrange("t p n -> p t n")).then_inc(mask_in, 16)
            sp.dma_start(pslot[0], a["W_skip"].rearrange("(c p) f -> p c f", p=128)).then_inc(skip_in, 16)
            sp.dma_start(bias_row[0:TP, :], a["b_skip"].partition_broadcast(TP)).then_inc(skip_in, 16)
            sp.wait_ge(skip_in, 32)
            stage_end(sp, 7)
            sp.dma_start(pslot[0], a["L2_WT"].rearrange("(c p) f -> p c f", p=128)).then_inc(w2_in, 16)
            sp.dma_start(bias_row[0:TP, :], a["L2_b"].partition_broadcast(TP)).then_inc(w2_in, 16)
            stage_end(sp, 8)
            sp.dma_start(QK[0:64, 0, :], a["noise"].partition_broadcast(64)).then_inc(noise_in, 16)
            sp.dma_start(M[0:TP, :, :], mask_dram.rearrange("t p n -> p t n")).then_inc(mask_in, 16)
            sp.dma_start(x3_dram, X[0:TP, :, :]).then_inc(x3_out, 16)
            sp.wait_ge(x3_out, 16)
            stage_end(sp, 9)
            with sp.Fori(0, BLOCKS) as b:
                def weight(slot, name):
                    sp.dma_start(wslot[slot], a[name][bass.ds(b, 1)].rearrange("a (c p) f -> p (a c) f", p=128)).then_inc(w_in[slot], 16)

                def condition(i):
                    sp.dma_start(cond_w[0], a[f"s{i}"][bass.ds(b, 1)].rearrange("a c f -> (a c) f")).then_inc(cond_in, 16)
                    sp.dma_start(cond_w[1], a[f"b{i}"][bass.ds(b, 1)].rearrange("a c f -> (a c) f")).then_inc(cond_in, 16)
                    sp.dma_start(bias3[0:TP, :], a[("bo", "m_b2")[i - 1]][bass.ds(b, 1)].rearrange("a f -> (a f)").partition_broadcast(TP)).then_inc(cond_in, 16)

                condition(1)
                weight(0, "wq")
                weight(1, "wk")
                weight(2, "wv")
                sp.dma_start(bv_all[0:TP, :], a["bv"][bass.ds(b, 1)].rearrange("a f -> (a f)").partition_broadcast(TP)).then_inc(bv_in, 16)
                loop_stage_end(sp, b, 0)
                sp.wait_ge(q_done, b * HEADS + HEADS)
                weight(0, "wo")
                sp.wait_ge(k_done, b * HEADS + HEADS)
                weight(1, "m_w1")
                sp.wait_ge(v_done, b * (3 * HEADS) + 3 * HEADS)
                weight(2, "m_w2")
                loop_stage_end(sp, b, 1)
                condition(2)
                loop_stage_end(sp, b, 2)
                loop_stage_end(sp, b, 3)
                loop_stage_end(sp, b, 4)
            x3v = PT[0:TP, 0:T * F]
            sp.dma_start(x3v, x3_dram).then_inc(x3_in, 16)
            sp.wait_ge(x_in, 32)
            sp.wait_ge(ln_step, LN3 + 6)
            sp.dma_start(out.rearrange("(t p) f -> p t f", p=TP), X[0:TP, :, :]).then_inc(out_done, 16)
            sp.wait_ge(out_done, 16)

        @block.gpsimd
        def _(pool):
            pool.iota(iota32[:, :], [[1, N]], base=0, channel_multiplier=0).then_inc(iota_done, 1)
            step = 0
            pool.wait_ge(iota_done, 2)
            pool.wait_ge(const_in, 16 * 18)
            for d in range(T):
                z, c1, o = gbuf[d % 2], gbuf[2 + d % 2], gbuf[6 + d % 2]
                pool.wait_ge(ct_copied, d + 1)
                if d >= 2:
                    pool.wait_ge(ln_done, d - 1)
                pool.tensor_copy(c1[0:TP, :], ct[d % 2][0:TP, :]).then_inc(loops_step, 1)
                pool.wait_ge(loops_step, 3 * d + 1)
                pool.tensor_tensor(c1[0:TP, TP * d:TP * (d + 1)], c1[0:TP, TP * d:TP * (d + 1)],
                                   ident[0:TP, 0:TP], ALU.add).then_inc(loops_step, 1)
                pool.wait_ge(loops_step, 3 * d + 2)
                pool.tensor_scalar(z[0:TP, :], c1[0:TP, :], 0.0, BIG, ALU.is_equal, ALU.mult).then_inc(loops_step, 1)
                pool.wait_ge(ln_done, d + 1)
                pool.wait_ge(loops_step, 3 * d + 3)
                if d >= 2:
                    pool.wait_ge(mask_t_out[d % 2], 16 * (d // 2))
                pool.tensor_tensor(o[0:TP, :], z[0:TP, :], gbuf[4 + d % 2][0:TP, :], ALU.subtract).then_inc(mask_t_ready, 1)
            stage_end(pool, 1)
            for t in range(T):
                c1 = gbuf[4 + t % 2]
                if t >= 2:
                    pool.wait_ge(cl_out[t % 2], 16 * (t // 2))
                pool.tensor_copy(c1[0:TP, :], M[0:TP, t, :]).then_inc(cl_step, 1)
                pool.wait_ge(cl_step, 2 * t + 1)
                pool.tensor_tensor(c1[0:TP, TP * t:TP * (t + 1)], c1[0:TP, TP * t:TP * (t + 1)],
                                   ident[0:TP, 0:TP], ALU.add).then_inc(cl_step, 1)
            stage_end(pool, 2)
            stage_end(pool, 3)
            stage_end(pool, 4)
            stage_end(pool, 5)
            with pool.Fori(0, H1 // 2) as pair:
                for e in range(2):
                    pool.wait_ge(acc_ready, pair * (2 * NG) + (A1 - NG + NG * e))
                    pool.tensor_copy(vh1[0:TP, e, :, :], H[0:TP, :, bass.ds(pair * 128 + C1 * e, C1)]).then_inc(vh1_ready[e], 1)
            stage_end(pool, 6)

            def add_bias(row, s):
                for t in range(T):
                    pool.tensor_tensor(X[0:TP, t, :], X[0:TP, t, :], row[0:TP, :], ALU.add).then_inc(s, 1)

            pool.wait_ge(skip_in, 32)
            add_bias(bias_row, bias_added)
            stage_end(pool, 7)
            stage_end(pool, 8)
            stage_end(pool, 9)
            with pool.Fori(0, BLOCKS) as b:
                pool.wait_ge(y_step, b * (4 * T) + 2 * T)
                pool.wait_ge(cond_in, b * 96 + 48)
                add_bias(bias3, bias3_added)
                loop_stage_end(pool, b, 0)
                loop_stage_end(pool, b, 1)
                loop_stage_end(pool, b, 2)
                pool.wait_ge(y_step, b * (4 * T) + 4 * T)
                pool.wait_ge(cond_in, b * 96 + 96)
                add_bias(bias3, bias3_added)
                loop_stage_end(pool, b, 3)
                loop_stage_end(pool, b, 4)

        @block.scalar
        def _(act):
            act.wait_ge(iota_done, 2)
            for d in range(T + 1):
                if d < T:
                    act.wait_ge(ct_counted, d + 1)
                    if d >= 2:
                        act.wait_ge(ct_turned, d - 1)
                        act.wait_ge(loops_step, 3 * (d - 2) + 1)
                    act.activation(ct[d % 2][0:TP, :], psA[0:TP, 0:N], ACT.Copy).then_inc(ct_copied, 1)
                if d < T:
                    act.wait_ge(loops_step, 3 * d + 2)
                    if d >= 2:
                        act.wait_ge(mask_t_ready, d - 1)
                    act.activation(gbuf[4 + d % 2][0:TP, :], gbuf[2 + d % 2][0:TP, :], ACT.Ln, bias=tiny[0:TP, :]).then_inc(ln_done, 1)
                if d >= 1:
                    act.wait_ge(ct_turned, d)
                    act.activation(M[0:TP, :, TP * (d - 1):TP * d], blocks_B[0:TP, :, 0:TP], ACT.Copy).then_inc(ct_placed, 1)
            stage_end(act, 1)
            for t in range(T):
                if t >= 2:
                    act.wait_ge(mask_ready, t - 1)
                act.activation(gbuf[t % 2][0:TP, :], M[0:TP, t, :], ACT.Ln, bias=tiny[0:TP, :]).then_inc(ln2_done, 1)
            stage_end(act, 2)

            def leaky(g, i, per, row, bias):
                at_least(act, turned, g + freed(i, per))
                settle(act)
                act.activation(slot(i), row[0:TP, :], ACT.Identity, bias=bias(i % T), scale=-1.0).then_inc(raw_ready, 1)

            def exponent(g, i):
                act.wait_ge(shifted, g + (i + 1))
                act.activation(slot(i), slot(i), ACT.Exp, bias=own(shift2, i), scale=-1.0, accum_out=own(den2, i)).then_inc(exped, 1)

            def place(g, at, i, per=1):
                t = i % T
                k = group_of(t)
                act.wait_ge(turned, g + (i + 1))
                if t == GROUPS[k][0]:
                    at_least(act, acc_ready, at + per * (k - 1))
                c = TP * (t - GROUPS[k][0])
                act.activation(pt[0:TP, k % 2, :, c:c + TP], blocks_B[0:TP, :, 0:TP], ACT.Copy).then_inc(placed, 1)

            def leaky_softmax(g, at, first, per, row, bias, jobs=1):
                leaky(g, first, per, row, bias)
                leaky(g, first + 1, per, row, bias)
                exponent(g, first)
                for i in range(first, first + T):
                    if i + 2 < first + T:
                        leaky(g, i + 2, per, row, bias)
                    if i + 1 < first + T:
                        exponent(g, i + 1)
                    place(g, at, i, jobs)

            def place_xt(base):
                for t in range(T):
                    act.wait_ge(xt_turned, base + t + 1)
                    act.activation(XT[:, :, TP * t:TP * (t + 1)],
                                   psB[:, BANK * (t % 2):BANK * (t % 2 + 1)].rearrange("p (c n) -> p c n", c=FC)[:, :, 0:TP],
                                   ACT.Copy).then_inc(xt_placed, 1)

            def row_std(n):
                act.wait_ge(ln_step, n)
                act.activation(rstd[0:TP, :], moments[0:TP, 0:T, 1], ACT.Sqrt, bias=eps[0:TP, :]).then_inc(ln_step, 1)

            act.wait_ge(trow_ready, 1)
            act.activation(QK[0:1, 1, :], psA[0:1, 0:N], ACT.Copy).then_inc(trow_copied, 1)
            act.wait_ge(trow_in, 16)
            act.wait_ge(scol_copied, 1)
            leaky_softmax(0, 0, 0, T, QK[:, 0, :], lambda t: neg_s[0:TP, t:t + 1], FC)
            stage_end(act, 3)
            with act.Fori(0, 2) as half:
                cols_h = bass.ds(half * HALF, HALF)
                act.wait_ge(basis_used, half * NB + 2)
                settle(act)
                act.activation(basis[0], OT[:, :, cols_h], ACT.Silu).then_inc(basis_ready, 1)
                for k in range(1, NB):
                    n = half * (NB - 1) + (k - 1)
                    act.wait_ge(basis_ready, half * NB + k)
                    settle(act)
                    act.activation(sp_u.rearrange("p (c n) -> p c n", c=FC), OT[:, :, cols_h], ACT.Abs,
                                   bias=centre[:, k - 1:k], scale=2.5).then_inc(abs_done, 1)
                    act.wait_ge(cut_done, 2 * n + 1)
                    act.activation(sp_a3, sp_a, ACT.Square, scale=6.0 ** -0.5).then_inc(square_done, 1)
                    act.wait_ge(cut_done, 2 * n + 2)
                    act.activation(sp_b3, sp_u, ACT.Square, scale=1.5 ** -0.5).then_inc(square_done, 1)
            row_std(3)
            stage_end(act, 4)
            place_xt(0)
            act.wait_ge(arow_ready, 1)
            act.activation(QK[0:H1, 0, :], psB[0:H1, 0:N], ACT.Copy).then_inc(arow_copied, 1)
            stage_end(act, 5)
            with act.Fori(0, H1 // 2) as pair:
                for e in range(2):
                    act.wait_ge(arow_in[e], pair * 16 + 16)
                    leaky_softmax(pair * (2 * T) + G1, pair * (2 * NG) + (A1 + NG * e), T * e, 2 * T, QK[:, e, :],
                                  lambda t: neg_ad[0:TP, t, bass.ds(pair * 2 + e, 1)])
            stage_end(act, 6)
            act.wait_ge(bn_step, 16)
            act.activation(rstd[:, 0:FC], moments[:, 0:FC, 1], ACT.Sqrt, bias=eps[:, :]).then_inc(bn_step, 1)
            act.wait_ge(bn_step, 17 + 4)
            for c in range(FC):
                act.activation(OT[:, c, :], OT[:, c, :], ACT.Gelu, bias=bn_shift[:, c:c + 1], scale=bn_scale[:, c:c + 1]).then_inc(gelu_done, 1)
            row_std(9)
            stage_end(act, 7)
            act.wait_ge(dis_step, T)
            act.activation(dis[0:TP, :], dis[0:TP, :], ACT.Sqrt).then_inc(dis_step, 1)
            place_xt(T)
            for t in range(T):
                act.wait_ge(agg_ready, t + 1)
                act.wait_ge(dis_step, 2 + T)
                if t >= 2:
                    act.wait_ge(agg_added, t - 1)
                act.activation(temp[t % 2][0:TP, :], acc[t % 2][0:TP, :], ACT.Relu, scale=dis[0:TP, t:t + 1]).then_inc(agg_relued, 1)
            row_std(15)
            stage_end(act, 8)
            act.wait_ge(ph_step, 8)
            act.activation(QK[0:64, 0, :], QK[0:64, 1, :], ACT.Sin).then_inc(sin_done, 1)
            act.wait_ge(c1_ready, 1)
            act.activation(SB[0:16, 0, :], psA[0:16, 0:N], ACT.Silu, bias=fb1[0:16, :]).then_inc(c1_done, 1)
            act.wait_ge(c2_ready, 1)
            act.wait_ge(ph_step, 9)
            act.activation(condT[0:16, :], psB[0:16, 0:N], ACT.Identity, bias=fb2[0:16, :]).then_inc(c2_done, 1)
            stage_end(act, 9)
            with act.Fori(0, BLOCKS) as b:
                row_std(b * 8 + 20)
                place_xt(b * (2 * T) + 2 * T)
                loop_stage_end(act, b, 0)
                def copy_q(h):
                    act.wait_ge(q_ready, b * HEADS + (h + 1))
                    settle(act)
                    act.activation(QK[:, 0, :], psA[:, 0:N], ACT.Identity, bias=neg_bq[:, bass.ds(b * HEADS + h, 1)], scale=-QSCALE).then_inc(q_done, 1)

                copy_q(0)
                g = b * (HEADS * T) + G3
                for h in range(HEADS):
                    at = b * (HEADS * NG) + (A3 + NG * h)
                    exponent(g, T * h)
                    for t in range(T):
                        if t + 1 < T:
                            exponent(g, T * h + t + 1)
                        if t == 8 and h + 1 < HEADS:
                            copy_q(h + 1)
                        place(g, at, T * h + t)
                loop_stage_end(act, b, 1)
                loop_stage_end(act, b, 2)
                row_std(b * 8 + 24)
                place_xt(b * (2 * T) + 3 * T)
                loop_stage_end(act, b, 3)
                for o in range(FC):
                    act.wait_ge(hid_ready, b * FC + (o + 1))
                    settle(act)
                    act.activation(OT[:, o, :], (psA, psB)[o % 2][:, 0:N], ACT.Relu, bias=bm1[:, bass.ds(b * FC + o, 1)]).then_inc(hid_done, 1)
                loop_stage_end(act, b, 4)
            row_std(LN3 + 3)

        @block.vector
        def _(dve):
            dve.wait_ge(edges_in, 16)
            dve.tensor_copy(src_f[0:TP, :], edge_i[0:TP, 0:EC]).then_inc(graph_dve, 1)
            dve.tensor_copy(dst_f[0:TP, :], edge_i[0:TP, EC:2 * EC]).then_inc(graph_dve, 1)
            dve.memset(zero_bf, 0.0)
            dve.memset(ones_bf, 1.0)
            dve.memset(tiny[:, :], TINY)
            dve.memset(eps[:, :], EPS)
            dve.wait_ge(graph_dve, 2)
            for d in range(T):
                dve.tensor_scalar(ge_bf[0:TP, d, :], dst_f[0:TP, :], float(TP * d), None, ALU.is_ge).then_inc(graph_dve, 1)
            dve.wait_ge(graph_dve, 2 + T)
            dve.tensor_tensor(in_tile[0:TP, 0:T - 1, :], ge_bf[0:TP, 0:T - 1, :], ge_bf[0:TP, 1:T, :], ALU.subtract).then_inc(graph_dve, 1)
            dve.tensor_copy(in_tile[0:TP, T - 1, :], ge_bf[0:TP, T - 1, :]).then_inc(graph_dve, 1)
            dve.wait_ge(graph_dve, 4 + T)
            dve.tensor_reduce(in_batch[0:TP, :], in_tile[0:TP, :, :].rearrange("p t (k u) -> p (t k) u", u=U), AX_X, ALU.max).then_inc(graph_dve, 1)
            dve.wait_ge(iota_done, 1)
            dve.tensor_copy(iota16[:, :], iota32[:, :]).then_inc(iota_done, 1)
            has, first, end, length = rows[:, 800:1200], rows[:, 1200:1200 + T], rows[:, 1220:1220 + T], rows[:, 1240:1240 + T]
            dve.wait_ge(memb_sum, 1)
            dve.wait_ge(const_in, 16 * 18)
            g = 5 + T
            dve.tensor_scalar(has, psC[0:1, 0:T * EB], 1.0, None, ALU.min).then_inc(graph_dve, 1)
            dve.wait_ge(graph_dve, g + 1)
            dve.tensor_tensor(rows[:, 0:400], has, rows[:, 0:400], ALU.mult).then_inc(graph_dve, 1)
            dve.tensor_tensor(rows[:, 400:800], has, rows[:, 400:800], ALU.mult).then_inc(graph_dve, 1)
            dve.wait_ge(graph_dve, g + 3)
            dve.tensor_reduce(first, rows[:, 0:400].rearrange("p (t k) -> p t k", t=T), AX_X, ALU.min).then_inc(graph_dve, 1)
            dve.tensor_reduce(end, rows[:, 400:800].rearrange("p (t k) -> p t k", t=T), AX_X, ALU.max).then_inc(graph_dve, 1)
            dve.wait_ge(graph_dve, g + 5)
            dve.tensor_scalar(first, first, float(EB - 1), None, ALU.add).then_inc(graph_dve, 1)
            dve.wait_ge(graph_dve, g + 6)
            dve.tensor_tensor(length, end, first, ALU.subtract).then_inc(graph_dve, 1)
            dve.wait_ge(graph_dve, g + 7)
            dve.tensor_scalar(length, length, 1.0, None, ALU.max).then_inc(graph_dve, 1)
            dve.wait_ge(graph_dve, g + 8)
            dve.tensor_copy(table[:, 0:T], first).then_inc(table_ready, 1)
            dve.tensor_copy(table[:, T:2 * T], length).then_inc(table_ready, 1)
            dve.wait_ge(table_ready, 2)
            for d in range(T):
                first_b = dve.value_load(table[0:1, d:d + 1], min_val=0, max_val=EB - 1)
                batches = dve.value_load(table[0:1, T + d:T + d + 1], min_val=1, max_val=EB)
                with dve.Fori(0, batches) as r:
                    b = nc.s_assert_within(first_b + r, 0, EB - 1, skip_runtime_bounds_check_because="first + batches is at most EB by construction")
                    for u in range(U):
                        chunk = b * U + u
                        dve.wait_ge(hot_used[d], r * U + u + 1)
                        dve.tensor_scalar(one_src[0:TP, u, :], iota16[0:TP, :], src_f[0:TP, bass.ds(chunk, 1)], None, ALU.is_equal)
                        dve.tensor_scalar(one_dst[0:TP, u, :], iota16[0:TP, TP * d:TP * (d + 1)], dst_f[0:TP, bass.ds(chunk, 1)], None,
                                          ALU.is_equal).then_inc(hot_ready[d], 1)
            stage_end(dve, 1)
            for t in range(T):
                z = gbuf[2 + t % 2]
                dve.tensor_scalar(z[0:TP, :], M[0:TP, t, :], 0.0, BIG, ALU.is_equal, ALU.mult).then_inc(zero2, 1)
                dve.wait_ge(zero2, t + 1)
                dve.wait_ge(ln2_done, t + 1)
                dve.wait_ge(cl_step, 2 * t + 1)
                dve.scalar_tensor_tensor(M[0:TP, t, :], gbuf[t % 2][0:TP, :], -1.0, z[0:TP, :], ALU.mult, ALU.add).then_inc(mask_ready, 1)
            stage_end(dve, 2)

            def shift(g, i, per, source, masks):
                dve.wait_ge(raw_ready, g + (i + 1))
                if source is None:
                    dve.scalar_tensor_tensor(slot(i), slot(i), SLOPE, slot(i), ALU.mult, ALU.min).then_inc(sloped, 1)
                    dve.wait_ge(sloped, g + (i + 1))
                else:
                    dve.wait_ge(turned, g + freed(i, per))
                if masks:
                    dve.wait_ge(mask_in, masks)
                settle(dve)
                dve.tensor_tensor_reduce(slot(i), slot(i) if source is None else source, M[0:TP, i % T, :], 1.0, NO_ROW,
                                         ALU.add, ALU.min, own(shift2, i)).then_inc(shifted, 1)

            def divide(g, i):
                dve.wait_ge(exped, g + (i + 1))
                dve.tensor_scalar(own(inv2, i), own(den2, i), 1e-30, None, ALU.max).then_inc(inv_step, 1)
                dve.wait_ge(inv_step, g * 2 + (2 * i + 1))
                dve.reciprocal(own(inv2, i), own(inv2, i)).then_inc(inv_step, 1)
                dve.wait_ge(inv_step, g * 2 + (2 * i + 2))
                dve.tensor_scalar(slot(i), slot(i), own(inv2, i), None, ALU.mult).then_inc(prob_ready, 1)

            def norm_rows(tiles, n):
                last = len(tiles) - 1
                dve.wait_ge(ln_step, n + 1)
                for i, t in enumerate(tiles):
                    ins = dve.bn_stats(stats[0:TP, i, :], X[0:TP, t, :])
                ins.then_inc(ln_step, 1)
                dve.wait_ge(ln_step, n + 2)
                for i, t in enumerate(tiles):
                    ins = dve.bn_aggr(moments[0:TP, i, :], stats[0:TP, i, :])
                ins.then_inc(ln_step, 1)
                dve.wait_ge(ln_step, n + 4)
                dve.reciprocal(rstd[0:TP, :], rstd[0:TP, :]).then_inc(ln_step, 1)
                dve.wait_ge(ln_step, n + 5)
                for i, t in enumerate(tiles):
                    ins = dve.tensor_scalar(X[0:TP, t, :], X[0:TP, t, :], moments[0:TP, i, 0:1], rstd[0:TP, i:i + 1], ALU.subtract, ALU.mult)
                ins.then_inc(ln_step, 1)

            dve.wait_ge(u_ready, 1)
            dve.tensor_copy(u_cols, psC[:, 0:8].rearrange("p (c k) -> p c k", c=FC)).then_inc(u_copied, 1)
            dve.wait_ge(scol_ready, 1)
            dve.tensor_scalar(neg_s[0:TP, :], psD[0:TP, 0:T], -1.0, None, ALU.mult).then_inc(scol_copied, 1)
            n_acc = [0]

            def take0():
                i = n_acc[0]
                k, c = divmod(i, FC)
                first, n = GROUPS[k]
                dve.wait_ge(acc_ready, i + 1)
                dve.tensor_copy(OT[:, c, TP * first:TP * (first + n)], acc[i % 2][:, 0:TP * n]).then_inc(acc_taken, 1)
                n_acc[0] += 1

            shift(0, 0, T, None, 0)
            shift(0, 1, T, None, 0)
            for t in range(T):
                divide(0, t)
                if t + 2 < T:
                    shift(0, t + 2, T, None, 0)
                if t >= 5:
                    take0()
                    take0()
            while n_acc[0] < A1:
                take0()
            stage_end(dve, 3)
            with dve.Fori(0, 2) as half:
                for k in range(1, NB):
                    n = half * (NB - 1) + (k - 1)
                    dve.wait_ge(abs_done, n + 1)
                    dve.tensor_scalar(sp_a, sp_u, 2.0, 2.0, ALU.min, ALU.subtract).then_inc(cut_done, 1)
                    dve.wait_ge(cut_done, 2 * n + 1)
                    dve.tensor_scalar(sp_u, sp_u, 1.0, 1.0, ALU.min, ALU.subtract).then_inc(cut_done, 1)
                    dve.wait_ge(square_done, 2 * n + 1)
                    dve.tensor_tensor(sp_a3, sp_a3, sp_a, ALU.mult).then_inc(cube_done, 1)
                    dve.wait_ge(square_done, 2 * n + 2)
                    dve.wait_ge(cut_done, 2 * n + 2)
                    dve.tensor_tensor(sp_b3, sp_b3, sp_u, ALU.mult).then_inc(cube_done, 1)
                    dve.wait_ge(basis_used, half * NB + k)
                    dve.wait_ge(cube_done, 2 * n + 2)
                    dve.tensor_tensor(basis[k % 3].rearrange("p c n -> p (c n)"), sp_b3, sp_a3, ALU.subtract).then_inc(basis_ready, 1)
                dve.wait_ge(basis_used, half * NB + (NB + 2))
                for i in range(HT):
                    bank = (psA[0:TP, 0:BANK], psA[0:TP, BANK:2 * BANK], psA[0:TP, 2 * BANK:3 * BANK], psC[0:TP, :], psD[0:TP, :])[i]
                    x = X[0:TP, bass.ds(half * HT + i, 1), :].rearrange("p a f -> p (a f)")
                    ins = dve.tensor_tensor(x, x, bank, ALU.add)
                    if i == HT - 1:
                        ins.then_inc(half_added, 1)
            dve.wait_ge(half_added, 3)
            dve.sem_inc(ln_step, 1)
            norm_rows(range(T), 0)
            dve.wait_ge(ln_step, 6)
            stage_end(dve, 4)
            dve.wait_ge(const_in, 16 * 18)
            for k in range(2):
                for c in range(FC):
                    dve.tensor_scalar(att16[:, c, H1 * k:H1 * (k + 1)], head_of[:, c, :], att_cols[:, k, c:c + 1], None, ALU.mult).then_inc(att_done, 1)
            dve.wait_ge(u16_ready, 1)
            dve.tensor_copy(u16[:, :, :], psA[:, 0:FC * 2 * H1].rearrange("p (c k) -> p c k", c=FC)).then_inc(u16_copied, 1)
            for t in range(T):
                dve.wait_ge(h_ready, t + 1)
                dve.tensor_copy(H[0:TP, t, :], acc[t % 2][0:TP, :]).then_inc(h_copied, 1)
            dve.wait_ge(ad_ready, 1)
            dve.tensor_scalar(neg_ad[0:TP, :, :], psA[0:TP, BANK:BANK + T * H1].rearrange("p (t h) -> p t h", t=T), -1.0, None, ALU.mult).then_inc(ad_done, 1)
            stage_end(dve, 5)
            with dve.Fori(0, H1 // 2) as pair:
                for e in range(2):
                    g, at, last = pair * (2 * T) + G1, pair * (2 * NG) + (A1 + NG * e), T * e + T
                    half_p = slice(C1 * e, C1 * (e + 1))

                    def take1(k):
                        first, n = GROUPS[k]
                        dve.wait_ge(acc_ready, at + (k + 1))
                        dve.tensor_scalar(OT[half_p, bass.ds(pair, 1), TP * first:TP * (first + n)].rearrange("p a n -> p (a n)"),
                                          acc[k % 2][half_p, 0:TP * n], gat_bias[half_p, bass.ds(pair, 1)], None, ALU.add).then_inc(acc_taken, 1)

                    shift(g, T * e, 2 * T, None, 16)
                    shift(g, T * e + 1, 2 * T, None, 16)
                    for i in range(T * e, last):
                        divide(g, i)
                        if i + 2 < last:
                            shift(g, i + 2, 2 * T, None, 16)
                        if i == T * e + 6:
                            take1(0)
                    for k in range(1, NG):
                        take1(k)
            stage_end(dve, 6)
            for c in range(FC):
                for i, (at, w) in enumerate(COLS):
                    dve.bn_stats(stats[:, 3 * c + i, :], OT[:, c, at:at + w]).then_inc(bn_step, 1)
            dve.wait_ge(bn_step, 12)
            for c in range(FC):
                dve.bn_aggr(moments[:, c, :], stats[:, 3 * c:3 * c + 3, :]).then_inc(bn_step, 1)
            dve.wait_ge(bn_step, 17)
            dve.reciprocal(rstd[:, 0:FC], rstd[:, 0:FC]).then_inc(bn_step, 1)
            dve.wait_ge(bn_step, 18)
            dve.tensor_tensor(bn_scale, rstd[:, 0:FC], gamma, ALU.mult).then_inc(bn_step, 1)
            dve.wait_ge(bn_step, 19)
            dve.tensor_tensor(bn_shift, moments[:, 0:FC, 0], bn_scale, ALU.mult).then_inc(bn_step, 1)
            dve.wait_ge(bn_step, 20)
            dve.tensor_tensor(bn_shift, beta, bn_shift, ALU.subtract).then_inc(bn_step, 1)
            dve.wait_ge(bias_added, T)
            for t in range(T):
                dve.wait_ge(skip_ready, t + 1)
                dve.tensor_tensor(X[0:TP, t, :], X[0:TP, t, :], acc[t % 2][0:TP, :], ALU.add).then_inc(skip_added, 1)
            dve.wait_ge(skip_added, T)
            dve.sem_inc(ln_step, 1)
            norm_rows(range(T), 6)
            dve.wait_ge(ln_step, 12)
            stage_end(dve, 7)
            dve.wait_ge(mask_in, 32)
            for t in range(T):
                dve.tensor_reduce(dis[0:TP, t:t + 1], M[0:TP, t, :], AX_X, ALU.add).then_inc(dis_step, 1)
            dve.wait_ge(dis_step, T + 1)
            dve.reciprocal(dis[0:TP, :], dis[0:TP, :]).then_inc(dis_step, 1)
            dve.wait_ge(dis_step, T + 2)
            dve.wait_ge(w2_in, 32)
            for t in range(T):
                dve.wait_ge(h2_ready, t + 1)
                dve.tensor_tensor(H[0:TP, t, :], acc[t % 2][0:TP, :], bias_row[0:TP, :], ALU.add).then_inc(h2_step, 1)
                dve.wait_ge(h2_step, t + 1)
                dve.tensor_scalar(H[0:TP, t, :], H[0:TP, t, :], dis[0:TP, t:t + 1], None, ALU.mult).then_inc(h2_done, 1)
            for t in range(T):
                dve.wait_ge(agg_relued, t + 1)
                dve.tensor_tensor(X[0:TP, t, :], X[0:TP, t, :], temp[t % 2][0:TP, :], ALU.add).then_inc(agg_added, 1)
            dve.wait_ge(agg_added, T)
            dve.sem_inc(ln_step, 1)
            norm_rows(range(T), 12)
            dve.wait_ge(ln_step, 18)
            stage_end(dve, 8)
            dve.wait_ge(const_in, 16 * 18)
            dve.tensor_scalar(neg_bq, neg_bq, -QSCALE, None, ALU.mult)
            noise, angle, turns = QK[0:64, 0, :], QK[0:64, 1, :], SB[0:64, 0, :]
            dve.wait_ge(noise_in, 16)
            dve.tensor_scalar(angle, noise, freq[0:64, 0:1], None, ALU.mult).then_inc(ph_step, 1)
            dve.wait_ge(ph_step, 1)
            dve.tensor_scalar(turns, angle, 1 / TWO_PI, freq[0:64, 1:2], ALU.mult, ALU.add).then_inc(ph_step, 1)
            dve.wait_ge(ph_step, 2)
            dve.tensor_scalar(turns, turns, MAGIC, MAGIC, ALU.add, ALU.subtract).then_inc(ph_step, 1)
            for i, part in enumerate(PI_PARTS):
                dve.wait_ge(ph_step, 3 + i)
                dve.scalar_tensor_tensor(angle, turns, -part, angle, ALU.mult, ALU.add).then_inc(ph_step, 1)
            dve.wait_ge(ph_step, 6)
            dve.tensor_scalar(angle, angle, freq[0:64, 2:3], 3.1415925, ALU.add, ALU.min).then_inc(ph_step, 1)
            dve.wait_ge(ph_step, 7)
            dve.tensor_scalar(angle, angle, -3.1415925, None, ALU.max).then_inc(ph_step, 1)
            dve.memset(condT[:, :], 1.0).then_inc(ph_step, 1)
            stage_end(dve, 9)
            with dve.Fori(0, BLOCKS) as b:
                def cond_norm(i):
                    n = b * 8 + (18 + 4 * i)
                    base = b * (2 * T) + T * i
                    for t in range(T):
                        ins = dve.bn_stats(stats[0:TP, t, :], X[0:TP, t, :])
                    ins.then_inc(ln_step, 1)
                    dve.wait_ge(ln_step, n + 1)
                    settle(dve)
                    for t in range(T):
                        ins = dve.bn_aggr(moments[0:TP, t, :], stats[0:TP, t, :])
                    ins.then_inc(ln_step, 1)
                    dve.wait_ge(ln_step, n + 3)
                    dve.reciprocal(rstd[0:TP, :], rstd[0:TP, :]).then_inc(ln_step, 1)
                    dve.wait_ge(ln_step, n + 4)
                    for t in range(T):
                        x, y = xn[t % 2][0:TP, :], yb[t % 2][0:TP, :]
                        dve.tensor_scalar(x, X[0:TP, t, :], moments[0:TP, t, 0:1], rstd[0:TP, t:t + 1], ALU.subtract, ALU.mult).then_inc(y_step, 1)
                        dve.wait_ge(y_step, (base + t) * 2 + 1)
                        dve.wait_ge(cond_ready, base + (t + 1))
                        dve.scalar_tensor_tensor(x, psA[0:TP, BANK * (t % 2):BANK * (t % 2 + 1)], 1.0, x, ALU.add, ALU.mult).then_inc(y_step, 1)
                        dve.wait_ge(y_step, (base + t) * 2 + 2)
                        dve.wait_ge(xt_turned, base + (2 * T + t - 1))
                        dve.tensor_tensor(y, x, acc[t % 2][0:TP, :], ALU.add).then_inc(y_ready, 1)

                def add_projection(i):
                    base = b * (2 * T) + T * i
                    for t in range(T):
                        dve.wait_ge(proj_ready, base + (t + 1))
                        dve.tensor_tensor(X[0:TP, t, :], X[0:TP, t, :], acc[t % 2][0:TP, :], ALU.add).then_inc(proj_added, 1)

                cond_norm(0)
                loop_stage_end(dve, b, 0)
                def copy_k(h):
                    dve.wait_ge(k_ready, b * HEADS + (h + 1))
                    dve.tensor_scalar(QK[:, 1, :], psA[:, 0:N], bk[:, bass.ds(b * HEADS + h, 1)], None, ALU.add).then_inc(k_done, 1)

                copy_k(0)
                g = b * (HEADS * T) + G3
                for h in range(HEADS):
                    at = b * (HEADS * NG) + (A3 + NG * h)

                    def take3(k):
                        first, n = GROUPS[k]
                        dve.wait_ge(acc_ready, at + (k + 1))
                        dve.tensor_copy(OT[:, h, TP * first:TP * (first + n)], acc[k % 2][:, 0:TP * n]).then_inc(acc_taken, 1)

                    shift(g, T * h, HEADS * T, psA[0:TP, 0:N], 48)
                    shift(g, T * h + 1, HEADS * T, psA[0:TP, 0:N], 48)
                    for i, tiles in enumerate(VALUE_TILES):
                        dve.wait_ge(v_ready, b * (3 * HEADS) + (3 * h + i + 1))
                        if h == 0 and i == 0:
                            dve.wait_ge(bv_in, b * 16 + 16)
                        for t in tiles:
                            ins = dve.tensor_tensor(vh[0:TP, t, :], acc[i % 2][0:TP, DH * (t % 4):DH * (t % 4 + 1)], bv_all[0:TP, DH * h:DH * (h + 1)], ALU.add)
                        ins.then_inc(v_done, 1)
                    for t in range(T):
                        divide(g, T * h + t)
                        if t + 2 < T:
                            shift(g, T * h + t + 2, HEADS * T, psA[0:TP, 0:N], 48)
                        if t == 6:
                            take3(0)
                    if h + 1 < HEADS:
                        copy_k(h + 1)
                    for k in range(1, NG):
                        take3(k)
                loop_stage_end(dve, b, 1)
                add_projection(0)
                loop_stage_end(dve, b, 2)
                cond_norm(1)
                loop_stage_end(dve, b, 3)
                add_projection(1)
                loop_stage_end(dve, b, 4)
            dve.wait_ge(x3_in, 16)
            dve.tensor_tensor(X[0:TP, :, :], X[0:TP, :, :], PT[0:TP, 0:T * F].rearrange("p (t f) -> p t f", t=T), ALU.add).then_inc(ln_step, 1)
            norm_rows(range(T), LN3)

        @block.tensor
        def _(pe):
            pe.wait_ge(graph_dve, 5 + T)
            pe.matmul(psC[0:1, 0:T * EB], ones_bf[0:TP, 0:1], in_batch[0:TP, :], start=True, stop=True).then_inc(memb_sum, 1)
            pe.wait_ge(table_ready, 2)
            pe.wait_ge(const_in, 16 * 18)
            pe.sem_inc(hot_used[0], U)

            def turn(d):
                pe.wait_ge(ct_copied, d + 1)
                if d >= 1:
                    pe.wait_ge(ct_placed, d)
                for j in range(T):
                    mm = pe.transpose(blocks_B[0:TP, j, 0:TP], ct[d % 2][0:TP, TP * j:TP * (j + 1)], ident[0:TP, 0:TP])
                mm.then_inc(ct_turned, 1)

            for d in range(T):
                if d >= 1:
                    pe.wait_ge(ct_copied, d)
                for c, w in COLS:
                    pe.matmul(psA[0:TP, c:c + w], zero_bf[0:TP, 0:TP], zero_bf[0:TP, 0:w], start=True, stop=False)
                batches = pe.value_load(table[0:1, T + d:T + d + 1], min_val=1, max_val=EB)
                with pe.Fori(0, batches) as r:
                    for u in range(U):
                        pe.wait_ge(hot_ready[d], r * U + u + 1)
                        for c, w in COLS:
                            mm = pe.matmul(psA[0:TP, c:c + w], one_dst[0:TP, u, :], one_src[0:TP, u, c:c + w], start=False, stop=False)
                        mm.then_inc(hot_used[d], 1)
                for c, w in COLS:
                    mm = pe.matmul(psA[0:TP, c:c + w], zero_bf[0:TP, 0:TP], zero_bf[0:TP, 0:w], start=False, stop=True)
                    if c == 0 and d + 1 < T:
                        mm.then_inc(hot_used[d + 1], U)
                mm.then_inc(ct_counted, 1)
                if d >= 1:
                    turn(d - 1)
            turn(T - 1)
            stage_end(pe, 1)
            stage_end(pe, 2)

            def turn_p(g, i):
                pe.wait_ge(prob_ready, g + (i + 1))
                at_least(pe, placed, g + i)
                for j in range(T):
                    mm = pe.transpose(blocks_B[0:TP, j, 0:TP], slot(i)[:, TP * j:TP * (j + 1)], ident[0:TP, 0:TP])
                mm.then_inc(turned, 1)

            def multiply(bank, k, values, js, out_p):
                n = GROUPS[k][1]
                for j in js:
                    mm = pe.matmul(acc[bank % 2][out_p, 0:TP * n], values(j), pt[0:TP, k % 2, j, 0:TP * n], start=(j == 0), stop=(j == T - 1))
                if js[-1] == T - 1:
                    mm.then_inc(acc_ready, 1)

            def turn_x(base):
                for t in range(T):
                    at_least(pe, xt_placed, base + t - 1)
                    for c in range(FC):
                        at = BANK * (t % 2) + 128 * c
                        mm = pe.transpose(psB[:, at:at + TP], X[0:TP, t, 128 * c:128 * (c + 1)], ident[0:TP, 0:TP])
                    mm.then_inc(xt_turned, 1)

            def tile_of(v, c, t):
                return v[:, c, TP * t:TP * (t + 1)]

            pe.wait_ge(w0_in, 16)
            pe.wait_ge(x_in, 32)
            for f in range(FC):
                for o in range(FC):
                    mm = pe.matmul(psC[:, 2 * f:2 * f + 2], wslot[0][:, o, 128 * f:128 * (f + 1)], a_cols[:, o, :], start=(o == 0), stop=(o == FC - 1))
            mm.then_inc(u_ready, 1)
            pe.wait_ge(u_copied, 1)
            for at, w in COLS:
                for f in range(FC):
                    mm = pe.matmul(psA[0:1, at:at + w], u_cols[:, f, 1:2], XT[:, f, at:at + w], start=(f == 0), stop=(f == FC - 1))
            mm.then_inc(trow_ready, 1)
            for t in range(T):
                for f in range(FC):
                    mm = pe.matmul(psD[0:TP, t:t + 1], tile_of(XT, f, t), u_cols[:, f, 0:1], start=(f == 0), stop=(f == FC - 1))
            mm.then_inc(scol_ready, 1)
            jobs = [(k, c) for k in range(NG) for c in range(FC)]

            def job0(i):
                k, c = jobs[i]
                pe.wait_ge(placed, GROUPS[k][0] + GROUPS[k][1])
                at_least(pe, acc_taken, i - 1)
                if i == 1:
                    pe.wait_ge(scol_copied, 1)
                multiply(i, k, lambda j: X[0:TP, j, 128 * c:128 * (c + 1)], range(T), slice(0, 128))

            for t in range(T):
                turn_p(0, t)
                if t >= 4:
                    job0(2 * (t - 4))
                    job0(2 * (t - 4) + 1)
            for i in range(2 * (T - 4), len(jobs)):
                job0(i)
            stage_end(pe, 3)
            pe.sem_inc(basis_used, 2)
            pe.sem_inc(half_added, 1)
            with pe.Fori(0, 2) as half:
                pe.wait_ge(half_added, half + 1)
                for k in range(NB):
                    pe.wait_ge(basis_ready, half * NB + (k + 1))
                    pe.wait_ge(spline_w_in[k % 3], half * 48 + 16 * (k // 3 + 1))
                    for i in range(HT):
                        bank = (psA[0:TP, 0:BANK], psA[0:TP, BANK:2 * BANK], psA[0:TP, 2 * BANK:3 * BANK], psC[0:TP, :], psD[0:TP, :])[i]
                        for c in range(FC):
                            mm = pe.matmul(bank, basis[k % 3][:, c, TP * i:TP * (i + 1)], pslot[k % 3][:, c, :],
                                           start=(k == 0 and c == 0), stop=(k == NB - 1 and c == FC - 1))
                    mm.then_inc(basis_used, 1)
            stage_end(pe, 4)
            turn_x(0)
            pe.wait_ge(gat_w_in, 32)
            pe.wait_ge(att_done, 8)
            for f in range(FC):
                for o in range(FC):
                    mm = pe.matmul(psA[:, 16 * f:16 * (f + 1)], pslot[1][:, o, 128 * f:128 * (f + 1)], att16[:, o, :], start=(o == 0), stop=(o == FC - 1))
            mm.then_inc(u16_ready, 1)
            pe.wait_ge(xt_placed, T)
            for t in range(T):
                if t >= 2:
                    pe.wait_ge(h_copied, t - 1)
                for f in range(FC):
                    mm = pe.matmul(acc[t % 2][0:TP, :], tile_of(XT, f, t), pslot[0][:, f, :], start=(f == 0), stop=(f == FC - 1))
                mm.then_inc(h_ready, 1)
            pe.wait_ge(u16_copied, 1)
            for at, w in COLS:
                for f in range(FC):
                    mm = pe.matmul(psB[0:H1, at:at + w], u16[:, f, 0:H1], XT[:, f, at:at + w], start=(f == 0), stop=(f == FC - 1))
            mm.then_inc(arow_ready, 1)
            for t in range(T):
                for f in range(FC):
                    mm = pe.matmul(psA[0:TP, BANK + H1 * t:BANK + H1 * (t + 1)], tile_of(XT, f, t), u16[:, f, H1:2 * H1], start=(f == 0), stop=(f == FC - 1))
            mm.then_inc(ad_ready, 1)
            stage_end(pe, 5)

            def part(g, at, k, values, js, out_p):
                if js[0] == 0:
                    pe.wait_ge(placed, g + (GROUPS[k][0] + GROUPS[k][1]))
                    pe.wait_ge(acc_taken, at + (k - 1))
                multiply(k, k, values, js, out_p)

            def head(g, first, at, values, out_p, before=lambda t: None):
                for t in range(T):
                    before(t)
                    turn_p(g, first + t)
                    if t in PARTS:
                        k, js = PARTS[t]
                        if t == 3:
                            before(None)
                        part(g + first, at, k, values, js, out_p)
                part(g + first, at, 2, values, range(4, T), out_p)
                part(g + first, at, 3, values, range(T), out_p)

            with pe.Fori(0, H1 // 2) as pair:
                for e in range(2):
                    pe.wait_ge(vh1_ready[e], pair + 1)
                    head(pair * (2 * T) + G1, T * e, pair * (2 * NG) + (A1 + NG * e), lambda j: vh1[0:TP, e, j, :], slice(C1 * e, C1 * (e + 1)))
            stage_end(pe, 6)
            pe.wait_ge(skip_in, 32)
            for t in range(T):
                if t >= 2:
                    pe.wait_ge(skip_added, t - 1)
                for f in range(FC):
                    pe.matmul(acc[t % 2][0:TP, :], tile_of(XT, f, t), pslot[0][:, f, :], start=(f == 0), stop=False)
                if t == 0:
                    pe.wait_ge(gelu_done, FC)
                for f in range(FC):
                    mm = pe.matmul(acc[t % 2][0:TP, 128 * f:128 * (f + 1)], tile_of(OT, f, t), ident[:, :], start=False, stop=(f == FC - 1))
                mm.then_inc(skip_ready, 1)
            stage_end(pe, 7)
            turn_x(T)
            pe.wait_ge(w2_in, 32)
            pe.wait_ge(xt_placed, 2 * T)
            for t in range(T):
                if t >= 2:
                    pe.wait_ge(h2_step, t - 1)
                for f in range(FC):
                    mm = pe.matmul(acc[t % 2][0:TP, :], tile_of(XT, f, t), pslot[0][:, f, :], start=(f == 0), stop=(f == FC - 1))
                mm.then_inc(h2_ready, 1)
            pe.wait_ge(h2_done, T)
            pe.wait_ge(mask_in, 32)
            for t in range(T):
                if t >= 2:
                    pe.wait_ge(agg_relued, t - 1)
                for j in range(T):
                    mm = pe.matmul(acc[t % 2][0:TP, :], M[0:TP, j, TP * t:TP * (t + 1)], H[0:TP, j, :], start=(j == 0), stop=(j == T - 1))
                mm.then_inc(agg_ready, 1)
            stage_end(pe, 8)
            pe.wait_ge(sin_done, 1)
            for at, w in COLS:
                mm = pe.matmul(psA[0:16, at:at + w], fw[0:64, 0:16], QK[0:64, 0, at:at + w], start=True, stop=True)
            mm.then_inc(c1_ready, 1)
            pe.wait_ge(c1_done, 1)
            for at, w in COLS:
                mm = pe.matmul(psB[0:16, at:at + w], fw[0:16, 16:32], SB[0:16, 0, at:at + w], start=True, stop=True)
            mm.then_inc(c2_ready, 1)
            stage_end(pe, 9)
            with pe.Fori(0, BLOCKS) as b:
                def condition_rows(i):
                    base = b * (2 * T) + T * i

                    def turn_y(t):
                        pe.wait_ge(y_ready, base + (t + 1))
                        pe.wait_ge(xt_placed, base + (2 * T + t - 1))
                        for c in range(FC):
                            at = BANK * (t % 2) + 128 * c
                            mm = pe.transpose(psB[:, at:at + TP], yb[t % 2][0:TP, 128 * c:128 * (c + 1)], ident[0:TP, 0:TP])
                        mm.then_inc(xt_turned, 1)

                    pe.wait_ge(cond_in, b * 96 + 48 * (i + 1))
                    for t in range(T):
                        if t >= 2:
                            pe.wait_ge(y_ready, base + (t - 1))
                        rows_t = condT[0:17, TP * t:TP * (t + 1)]
                        pe.matmul(psA[0:TP, BANK * (t % 2):BANK * (t % 2 + 1)], rows_t, cond_w[0], start=True, stop=True)
                        pe.matmul(acc[t % 2][0:TP, :], rows_t, cond_w[1], start=True, stop=True).then_inc(cond_ready, 1)
                        if t >= 1:
                            turn_y(t - 1)
                    turn_y(T - 1)

                def project(i, source, w):
                    base = b * (2 * T) + T * i
                    for t in range(T):
                        if t >= 2:
                            pe.wait_ge(proj_added, base + (t - 1))
                        for f in range(FC):
                            mm = pe.matmul(acc[t % 2][0:TP, :], tile_of(source, f, t), w[:, f, :], start=(f == 0), stop=(f == FC - 1))
                        mm.then_inc(proj_ready, 1)

                condition_rows(0)
                loop_stage_end(pe, b, 0)
                def project_head(h, s):
                    if h == 0:
                        pe.wait_ge(w_in[s], b * 32 + 16)
                    if s == 0:
                        pe.wait_ge(shifted, b * (HEADS * T) + (G3 + T * h))
                    else:
                        pe.wait_ge(q_done, b * HEADS + (h + 1))
                    for c0, w0 in COLS:
                        for f in range(FC):
                            mm = pe.matmul(psA[:, c0:c0 + w0], wslot[s][:, f, DH * h:DH * (h + 1)], XT[:, f, c0:c0 + w0], start=(f == 0), stop=(f == FC - 1))
                    mm.then_inc((q_ready, k_ready)[s], 1)

                project_head(0, 0)
                project_head(0, 1)
                g = b * (HEADS * T) + G3
                for h in range(HEADS):
                    at = b * (HEADS * NG) + (A3 + NG * h)

                    def scores(t):
                        if t == 0:
                            pe.wait_ge(k_done, b * HEADS + (h + 1))
                        pe.wait_ge(shifted, g + (T * h + t))
                        for c0, w0 in COLS:
                            mm = pe.matmul(psA[0:TP, c0:c0 + w0], QK[:, 0, TP * t:TP * (t + 1)], QK[:, 1, c0:c0 + w0], start=True, stop=True)
                        mm.then_inc(raw_ready, 1)

                    def before(t):
                        if t is None:
                            pe.wait_ge(v_done, b * (3 * HEADS) + (3 * h + 3))
                        elif t + 2 < T:
                            scores(t + 2)
                        elif h + 1 < HEADS:
                            project_head(h + 1, t - 8)

                    scores(0)
                    scores(1)
                    if h == 0:
                        pe.wait_ge(w_in[2], b * 32 + 16)
                    for i, tiles in enumerate(VALUE_TILES):
                        if i < 2:
                            pe.wait_ge(acc_taken, at + (i - 1))
                        else:
                            pe.wait_ge(v_done, b * (3 * HEADS) + (3 * h + 1))
                        for t in tiles:
                            for f in range(FC):
                                mm = pe.matmul(acc[i % 2][0:TP, DH * (t % 4):DH * (t % 4 + 1)], tile_of(XT, f, t), wslot[2][:, f, DH * h:DH * (h + 1)], start=(f == 0), stop=(f == FC - 1))
                        mm.then_inc(v_ready, 1)
                    head(g, T * h, at, lambda j: vh[0:TP, j, :], slice(0, 128), before)
                loop_stage_end(pe, b, 1)
                pe.wait_ge(w_in[0], b * 32 + 32)
                project(0, OT, wslot[0])
                loop_stage_end(pe, b, 2)
                condition_rows(1)
                loop_stage_end(pe, b, 3)
                pe.wait_ge(w_in[1], b * 32 + 32)
                for o in range(FC):
                    if o >= 2:
                        pe.wait_ge(hid_done, b * FC + (o - 1))
                    for c0, w0 in COLS:
                        for f in range(FC):
                            mm = pe.matmul((psA, psB)[o % 2][:, c0:c0 + w0], wslot[1][:, f, 128 * o:128 * (o + 1)], XT[:, f, c0:c0 + w0], start=(f == 0), stop=(f == FC - 1))
                    mm.then_inc(hid_ready, 1)
                pe.wait_ge(hid_done, b * FC + FC)
                pe.wait_ge(w_in[2], b * 32 + 32)
                project(1, OT, wslot[2])
                loop_stage_end(pe, b, 4)


def kernel(**inputs):
    from concourse import bacc, mybir as _mybir
    from concourse.bass_utils import run_bass_kernel_spmd

    g = {k: np.asarray(v) for k, v in inputs.items()}

    def cols_of(v):
        return v.reshape(-1, 128).T

    arrays = dict(shape_constants())
    arrays["x"] = g["x"]
    arrays["xT"] = g["x"].T
    arrays["edges"] = np.concatenate([g["src"].reshape(EC, TP).T, g["dst"].reshape(EC, TP).T], axis=1)
    arrays["L0_a"] = g["L0_gnn_a"].reshape(2, FC, 128).transpose(2, 1, 0)
    arrays["att"] = np.stack([g["L1_gnn_att_src"].reshape(FC, 128), g["L1_gnn_att_dst"].reshape(FC, 128)]).transpose(2, 0, 1)
    arrays["gat_bias"] = cols_of(g["L1_gnn_gat_bias"])
    arrays["gamma"] = cols_of(g["L1_gnn_bn_gamma"])
    arrays["beta"] = cols_of(g["L1_gnn_bn_beta"])
    for name, key in (("bq", "bq"), ("bk", "bk"), ("bm1", "m_b1")):
        arrays[name] = cols_of(g["L3_gnn_" + key].reshape(-1))
    arrays["f_b1"] = g["L3_gnn_f_b1"].reshape(16, 1)
    arrays["f_b2"] = g["L3_gnn_f_b2"].reshape(16, 1)
    arrays["f_w1"] = g["L3_gnn_f_w1"]
    arrays["f_w2"] = g["L3_gnn_f_w2"]
    arrays["L0_WT"] = g["L0_gnn_W"].T
    bases = np.concatenate([g["L0_gnn_base_w"][:, :, None], g["L0_gnn_spline_w"]], axis=2)
    arrays["spline_w"] = bases.transpose(2, 1, 0).reshape(NB, FC, 128, F).transpose(0, 2, 1, 3)
    arrays["W_gat"], arrays["W_gatT"] = g["L1_gnn_W_gat"], g["L1_gnn_W_gat"].T
    arrays["W_skip"], arrays["b_skip"] = g["L1_gnn_W_skip"], g["L1_gnn_b_skip"]
    arrays["L2_WT"], arrays["L2_b"] = g["L2_gnn_W"].T, g["L2_gnn_b"]
    arrays["noise"] = g["node_vec1"].reshape(N)
    for i in (1, 2):
        for x in "sb":
            arrays[f"{x}{i}"] = np.concatenate([g[f"L3_gnn_{x}{i}_w"], g[f"L3_gnn_{x}{i}_b"][:, None]], axis=1)
    for k in ("wq", "wk", "wv", "wo", "m_w1", "m_w2", "bv", "bo", "m_b2"):
        arrays[k] = g["L3_gnn_" + k]
    arrays = {k: np.ascontiguousarray(v) for k, v in arrays.items()}

    nc = bacc.Bacc("TRN2", target_bir_lowering=False, num_devices=1)
    aps = {k: nc.dram_tensor("in_" + k, v.shape, _mybir.dt.from_np(v.dtype), kind="ExternalInput").ap()
           for k, v in arrays.items()}
    out = nc.dram_tensor("out", (N, F), F32, kind="ExternalOutput").ap()
    program(nc, aps, out)
    r = run_bass_kernel_spmd(nc, [{"in_" + k: v for k, v in arrays.items()}], core_ids=[0])
    return r.results[0]["out"]
```
